# Optimizing a Trainium2 kernel written in Bass

```python
import numpy as np
import jax
import jax.numpy as jnp

def _softmax(x, axis=-1):
    return jax.nn.softmax(x, axis=axis)

def _gelu(x):
    return jax.nn.gelu(x, approximate=True)

def _silu(x):
    return jax.nn.silu(x)

def _sigmoid(x):
    return jax.nn.sigmoid(x)

def _layernorm(x, axis=-1, eps=1e-05):
    m = jnp.mean(x, axis=axis, keepdims=True)
    v = jnp.var(x, axis=axis, keepdims=True)
    return (x - m) / jnp.sqrt(v + eps)

def _scatter_add(tgt, idx, src, axis=0):
    return tgt.at[idx].add(src)

def _segment_sum(src, seg, n):
    return jax.ops.segment_sum(src, seg, n)
kernel_name = 'mk_cond_resid_d2_seqx_r4_3e1035'

def setup_inputs(seed: int=0):
    np.random.seed(seed)
    _w = jnp.asarray

    def _rec_inputs():
        import jax
        import jax.numpy as jnp
        _rk = jax.random.key(seed)
        x = -0.000125 + 0.9999 * jax.random.normal(jax.random.fold_in(_rk, 1), (128, 64, 256), jnp.float32)
        _lenS = 64 - jax.random.randint(jax.random.fold_in(_rk, 7), (128,), 0, max(1, 64 // 4) + 1, jnp.int32)
        _lenS2 = 64 - jax.random.randint(jax.random.fold_in(_rk, 8), (128,), 0, max(1, 64 // 4) + 1, jnp.int32)
        itok_B_0_30 = jax.random.randint(jax.random.fold_in(_rk, 11), (128,), 0, 31, jnp.int32)
        itok_B_0_63 = jax.random.randint(jax.random.fold_in(_rk, 12), (128,), 0, 64, jnp.int32)
        return (x, itok_B_0_30, itok_B_0_63)
    x, itok_B_0_30, itok_B_0_63 = _rec_inputs()

    def _L0_cond_setup():
        import jax, jax.numpy as jnp
        import numpy as np
        C, I, O = (32, 256, 256)
        B, T = (64, 128)
        key = jax.random.key(seed)
        kx, kc, kw, kb = jax.random.split(key, 4)
        x = jax.random.normal(kx, (B, T, I), dtype=jnp.float32)
        cat_ids = jax.random.randint(kc, (B,), 0, C)
        W = 0.02 * jax.random.normal(kw, (C, I, O), dtype=jnp.float32)
        b = jnp.zeros((C, O), dtype=jnp.float32)
        return {'x': x, 'cat_ids': cat_ids, 'W': W, 'b': b}
    _L0_cond_all = _L0_cond_setup()
    _L0_cond_in = {k: v for k, v in _L0_cond_all.items() if k in ('W', 'b')}
    del _L0_cond_all

    def _L1_cond_setup():
        import jax, jax.numpy as jnp
        import numpy as np
        NUM_CATEGORIES = 64
        INPUT_DIM = 256
        HIDDEN_DIM = 256
        B = 64
        S = 64
        key = jax.random.key(seed)
        kx, kc, kw = jax.random.split(key, 3)
        x = jax.random.normal(kx, (B, S, INPUT_DIM), dtype=jnp.float32)
        cat_ids = jax.random.randint(kc, (B,), 0, NUM_CATEGORIES, dtype=jnp.int32)
        W = 0.02 * jax.random.normal(kw, (NUM_CATEGORIES, INPUT_DIM, HIDDEN_DIM), dtype=jnp.float32)
        b = jnp.zeros((NUM_CATEGORIES, HIDDEN_DIM), dtype=jnp.float32)
        return {'x': x, 'cat_ids': cat_ids, 'W': W, 'b': b}
    _L1_cond_all = _L1_cond_setup()
    _L1_cond_in = {k: v for k, v in _L1_cond_all.items() if k in ('W', 'b')}
    del _L1_cond_all
    return {'x': x, 'itok_B_0_30': itok_B_0_30, 'itok_B_0_63': itok_B_0_63, 'L0_cond_W': _L0_cond_in['W'], 'L0_cond_b': _L0_cond_in['b'], 'L1_cond_W': _L1_cond_in['W'], 'L1_cond_b': _L1_cond_in['b']}

def reference(x, itok_B_0_30, itok_B_0_63, L0_cond_W, L0_cond_b, L1_cond_W, L1_cond_b):
    import jax
    import jax.numpy as jnp

    def _L0_cond_ref(x, cat_ids, W, b):
        import jax, jax.numpy as jnp
        import numpy as np
        C, I, O = (32, 256, 256)
        B, T = (64, 128)
        selected_W = W[cat_ids]
        selected_b = b[cat_ids]
        if x.ndim == 2:
            return jnp.einsum('bi,bio->bo', x, selected_W) + selected_b
        return jnp.einsum('bti,bio->bto', x, selected_W) + selected_b[:, None, :]

    def _L1_cond_ref(x, cat_ids, W, b):
        import jax, jax.numpy as jnp
        import numpy as np
        NUM_CATEGORIES = 64
        INPUT_DIM = 256
        HIDDEN_DIM = 256
        B = 64
        S = 64
        selected_W = W[cat_ids]
        selected_b = b[cat_ids]
        out = jnp.einsum('bsd,bdh->bsh', x, selected_W) + selected_b[:, None, :]
        return out
    x = x + _L0_cond_ref(x, itok_B_0_30, L0_cond_W, L0_cond_b)
    x = x + _L1_cond_ref(x, itok_B_0_63, L1_cond_W, L1_cond_b)
    return x

_drawn_inputs = setup_inputs


def setup_inputs(seed=0):
    import zlib

    import numpy as np

    out = dict(_drawn_inputs(seed))
    spreads = {'L0_cond_b': (0.0, 0.1), 'L1_cond_b': (0.0, 0.1)}
    factors = {}
    for name, (base, spread) in spreads.items():
        noise = np.random.default_rng([zlib.crc32(name.encode()), seed]).standard_normal(out[name].shape)
        drawn = base * np.exp(spread * noise) if base else spread * noise
        out[name] = jnp.asarray(drawn.astype(out[name].dtype))
    for name, factor in factors.items():
        out[name] = (out[name] * factor).astype(out[name].dtype)
    return out
```

```python
from contextlib import ExitStack

import numpy as np

import concourse.bass as bass
from concourse import mybir

BATCHES, TOK, DIM = 128, 64, 256
CATS0, CATS1 = 32, 64
P = 128
CHUNKS = DIM // P
PAIRS = BATCHES // 2
WEIGHTS = CATS0 + CATS1
EARLY = 8
LANES = 8
STEP = 4
GROUP = 2
GROUPS = PAIRS // GROUP
ROUNDS = PAIRS // STEP
ENTRY = 6
SCORE, NEED, IOTA = 0, BATCHES, 2 * BATCHES
TIE = IOTA + WEIGHTS
CAT, INDEX, MASK = TIE + 1, TIE + 2, TIE + 3
CONSTS = MASK + 2


def constants():
    c = np.zeros((P, CONSTS), np.float32)
    w = np.arange(WEIGHTS)
    j = np.arange(BATCHES)
    layer = np.where(w < CATS1, 1, 0)
    c[:WEIGHTS, SCORE:SCORE + BATCHES] = 2 * BATCHES - 2 * j[None, :] - layer[:, None]
    pair, lay = np.divmod(np.arange(2 * PAIRS), 2)
    c[:, NEED:NEED + 2 * PAIRS] = (2 * BATCHES - 2 * (2 * pair + 1) - lay)[None, :] * P - 100
    c[:, IOTA:IOTA + WEIGHTS] = w[None, :]
    c[:WEIGHTS, TIE] = -w
    early = np.arange(EARLY)
    c[CATS1 + early, TIE] = 65536.0 * (EARLY - early)
    c[:WEIGHTS, CAT] = np.where(w < CATS1, w, w - CATS1)
    c[:WEIGHTS, INDEX] = w
    c[:WEIGHTS, MASK] = w >= CATS1
    c[:WEIGHTS, MASK + 1] = w < CATS1
    pick = np.zeros((96, 32), np.float32)
    pick[np.arange(96), np.arange(96) % 32] = 1
    return c, np.eye(P, dtype=np.float32), pick


def two_layers(nc, x, ids0, ids1, weights, biases, consts, eye, picks, out):
    fp32, bf16, i32 = mybir.dt.float32, mybir.dt.bfloat16, mybir.dt.int32
    ALU, AX = mybir.AluOpType, mybir.AxisListType
    ds = bass.ds

    x_d = x.rearrange("(g k h) r f -> g (h r) k f", k=GROUP, h=2)
    out_d = out.rearrange("(g k h) r f -> g (h r) k f", k=GROUP, h=2)
    w_d = weights.rearrange("w (p t) o -> w p (t o)", t=CHUNKS)

    with ExitStack() as ctx:
        def sb(name, shape, dt=fp32):
            return ctx.enter_context(nc.sbuf_tensor(name, shape, dt))

        def sem(name):
            return ctx.enter_context(nc.semaphore(name))

        w_all = sb("w_all", [P, WEIGHTS, CHUNKS * DIM])
        w0_b = sb("w0_b", [P, 2, CHUNKS * DIM])
        w1_b = sb("w1_b", [P, 2, CHUNKS * DIM])
        x_in = sb("x_in", [P, STEP, DIM])
        x_t = sb("x_t", [P, 2, CHUNKS, P])
        z = sb("z", [P, STEP, DIM])
        y_t = sb("y_t", [P, 2, CHUNKS, P])
        o = sb("o", [P, STEP, DIM])
        b0_t = sb("b0_t", [P, CHUNKS, BATCHES])
        b_sum = sb("b_sum", [96, 4, DIM], bf16)
        pick_b = sb("pick_b", [96, 32], bf16)
        pick = sb("pick", [96, 2, P], bf16)
        ident = sb("ident", [P, P])
        table = sb("table", [1, PAIRS * ENTRY], i32)
        order = sb("order", [1, WEIGHTS], i32)

        o_flat = o[:, :, :].rearrange("p s f -> p (s f)")
        z_flat = z[:, :, :].rearrange("p s f -> p (s f)")
        con = o_flat[:, 0:CONSTS]
        ids_i = o_flat[0:WEIGHTS, 384:512].bitcast(i32)
        ids_f = o_flat[0:WEIGHTS, 512:640]
        hot = o_flat[0:WEIGHTS, 640:768]
        scored = o_flat[0:WEIGHTS, 768:896]
        diag = o_flat[0:WEIGHTS, 896:992]
        best = o_flat[0:WEIGHTS, 992:993]
        key = o_flat[0:WEIGHTS, 993:994]
        rank = o_flat[0:WEIGHTS, 994:995]
        rank2 = o_flat[0:WEIGHTS, 995:997]
        needed = z_flat[0:WEIGHTS, 0:128]
        later = z_flat[0:WEIGHTS, 128:224]
        placed = z_flat[0:WEIGHTS, 256:352]
        ones = z_flat[0:WEIGHTS, 384:480]
        pick_f = z_flat[0:96, 480:512]
        b_all = z_flat[0:WEIGHTS, 512:768]

        ps = ctx.enter_context(nc.psum_tensor("ps", [P, 8, 512], fp32))
        ps_1, ps_2 = ps[:, 0:2, 0:DIM], ps[:, 2:4, 0:DIM]
        ps_x, ps_z = ps[:, 4:6, 0:DIM], ps[:, 6:8, 0:DIM]
        ps_keys = ps[0:WEIGHTS, 6, 0:WEIGHTS]
        ps_order = ps[0:1, 7, 0:WEIGHTS]
        ps_table = ps[0:1, 1, 0:PAIRS * ENTRY].rearrange("o (p k) -> o p k", k=ENTRY)
        ps_b0 = ps[:, 6, 0:2 * BATCHES].rearrange("p (t j) -> p t j", t=CHUNKS)
        ps_b = ps[0:96, 2:4, :].rearrange("p a (b f) -> p (a b) f", f=DIM)

        consts_in, ids_in, pick_in, biases_in, eye_in = (
            sem("consts_in"), sem("ids_in"), sem("pick_in"), sem("biases_in"), sem("eye_in"))
        prep = sem("prep")
        keys_out, order_out, table_out, b0_out, b_out = (
            sem("keys_out"), sem("order_out"), sem("table_out"), sem("b0_out"), sem("b_out"))
        order_ready, table_ready = sem("order_ready"), sem("table_ready")
        b0_ready, b_ready = sem("b0_ready"), sem("b_ready")
        w_lane = [sem(f"w_lane{i}") for i in range(LANES)]
        w_here = sem("w_here")
        x_here = [sem(f"x_here{i}") for i in range(2)]
        o_gone = [sem(f"o_gone{i}") for i in range(2)]
        tx_done, xt_ready = sem("tx_done"), sem("xt_ready")
        w0b_ready, w1b_ready = sem("w0b_ready"), sem("w1b_ready")
        l1_done, z_ready, tz_done, yt_ready = (
            sem("l1_done"), sem("z_ready"), sem("tz_done"), sem("yt_ready"))
        l2_done, o_ready = sem("l2_done"), sem("o_ready")

        block = ctx.enter_context(nc.Block())

        def whole(eng, step):
            for n in range(STEP):
                step(0, n)
            with eng.Fori(1, ROUNDS - 1) as r:
                for n in range(STEP):
                    step(r, n)
            for n in range(STEP):
                step(ROUNDS - 1, n)

        def pair(r, n, plus=0):
            return r + (n + plus) // STEP, (n + plus) % STEP

        def is_pair(r, n, p):
            return isinstance(r, int) and r * STEP + n == p

        @block.sync
        def _(sp):
            sp.dma_start(con, consts[:, :]).then_inc(consts_in, 16)
            sp.dma_start(o_flat[0:CATS1, 384:512].bitcast(i32),
                         ids1.rearrange("(a j) -> a j", a=1).to_broadcast([CATS1, BATCHES])
                         ).then_inc(ids_in, 16)
            sp.dma_start(o_flat[CATS1:WEIGHTS, 384:512].bitcast(i32),
                         ids0.rearrange("(a j) -> a j", a=1).to_broadcast([CATS0, BATCHES])
                         ).then_inc(ids_in, 16)
            sp.dma_start(b_all, biases[:, :]).then_inc(biases_in, 16)
            sp.dma_start(pick_f, picks[:, :]).then_inc(pick_in, 16)
            for k in range(EARLY):
                sp.dma_start(w_all[:, k, :], w_d[CATS1 + k]).then_inc(w_lane[k], 16)
            sp.wait_ge(order_ready, 1)
            with sp.Fori(EARLY // LANES, WEIGHTS // LANES) as turn:
                for lane in range(LANES):
                    which = sp.value_load(order[0:1, ds(turn * LANES + lane, 1)],
                                          min_val=0, max_val=WEIGHTS - 1)
                    sp.wait_ge(w_lane[lane], turn * 16)
                    sp.dma_start(w_all[:, ds(turn * LANES + lane, 1), :],
                                 w_d[ds(which, 1), :, :].rearrange("a p n -> p a n")
                                 ).then_inc(w_lane[lane], 16)

        @block.gpsimd
        def _(pool):
            with pool.Fori(0, WEIGHTS // LANES) as turn:
                for lane in range(LANES):
                    pool.wait_ge(w_lane[lane], turn * 16 + 16)
                    pool.sem_inc(w_here, 1)

        @block.tensor
        def _(pe):
            def transpose_x(r, n):
                if n % GROUP == 0:
                    pe.wait_ge(x_here[n // GROUP], r * 16 + 16)
                for t in range(CHUNKS):
                    last = nc.tensor.transpose(ps_x[:, n % 2, t * P:(t + 1) * P],
                                               x_in[:, n, t:DIM:CHUNKS], ident[:, :])
                last.then_inc(tx_done, 1)

            def layer(n, acts, copies, place, bank, fresh):
                for t in range(CHUNKS):
                    cols = slice(t * DIM, (t + 1) * DIM)
                    nc.tensor.matmul(bank[0:TOK, n % 2, :], acts[:, n % 2, t, 0:TOK],
                                     w_all[:, ds(place, 1), cols],
                                     start=fresh and t == 0, stop=t == CHUNKS - 1,
                                     skip_group_check=True)
                    last = nc.tensor.matmul(bank[TOK:P, n % 2, :], acts[:, n % 2, t, TOK:P],
                                            copies[:, n % 2, cols],
                                            start=fresh and t == 0, stop=t == CHUNKS - 1,
                                            skip_group_check=True)
                return last

            def place_of(r, n, which):
                return pe.value_load(table[0:1, ds(r * (STEP * ENTRY) + (n * ENTRY + which), 1)],
                                     min_val=0, max_val=WEIGHTS - 1)

            def layer_1(r, n):
                place = place_of(r, n, 2)
                pe.wait_ge(w0b_ready, r * STEP + (n + 1))
                pe.wait_ge(xt_ready, r * STEP + (n + 1))
                layer(n, x_t, w0_b, place, ps_1, True).then_inc(l1_done, 1)

            def layer_2(r, n):
                place = place_of(r, n, 3)
                pe.wait_ge(w1b_ready, r * STEP + (n + 1))
                pe.wait_ge(yt_ready, r * STEP + (n + 1))
                if is_pair(r, n, 0):
                    pe.wait_ge(b_ready, 1)
                nc.tensor.matmul(ps_2[:, n % 2, :], pick[:, n % 2, :], b_sum[:, ds(r // 4, 1), :],
                                 start=True, stop=False, skip_group_check=True)
                layer(n, y_t, w1_b, place, ps_2, False).then_inc(l2_done, 1)

            def transpose_z(r, n):
                pe.wait_ge(z_ready, r * STEP + (n + 1))
                for t in range(CHUNKS):
                    last = nc.tensor.transpose(ps_z[:, n % 2, t * P:(t + 1) * P],
                                               z[:, n, t:DIM:CHUNKS], ident[:, :])
                last.then_inc(tz_done, 1)

            pe.wait_ge(prep, 7)
            nc.tensor.matmul(ps_keys, ones, diag, start=True, stop=True).then_inc(keys_out, 1)
            pe.wait_ge(prep, 12)
            nc.tensor.matmul(ps_order, con[0:WEIGHTS, INDEX:INDEX + 1], placed,
                             start=True, stop=True).then_inc(order_out, 1)
            nc.tensor.matmul(ps_table[:, :, 0:2], ones[:, 0:1], needed, start=True, stop=True,
                             skip_group_check=True)
            for layer_n in range(2):
                last = nc.tensor.matmul(ps_table[:, :, 2 + layer_n:ENTRY:2],
                                        rank2[:, layer_n:layer_n + 1], hot,
                                        start=True, stop=True, skip_group_check=True)
            last.then_inc(table_out, 1)
            pe.wait_ge(eye_in, 16)
            transpose_x(0, 0)
            pe.wait_ge(biases_in, 16)
            for t in range(CHUNKS):
                last = nc.tensor.matmul(ps_b0[:, t, :], b_all[CATS1:WEIGHTS, t:DIM:CHUNKS],
                                        hot[CATS1:WEIGHTS, :], start=True, stop=True,
                                        skip_group_check=True)
            last.then_inc(b0_out, 1)
            for g in range(4):
                for part in range(3):
                    last = nc.tensor.matmul(ps_b[32 * part:32 * part + 32, g, :],
                                            hot[:, 32 * g:32 * g + 32], b_all,
                                            start=True, stop=True, skip_group_check=True)
            last.then_inc(b_out, 1)
            pe.wait_ge(table_ready, 1)

            def step(r, n):
                layer_1(r, n)
                if not is_pair(r, n, PAIRS - 1):
                    transpose_x(*pair(r, n, 1))
                if not is_pair(r, n, 0):
                    layer_2(*pair(r, n, -1))
                transpose_z(r, n)

            whole(pe, step)
            layer_2(ROUNDS - 1, STEP - 1)

        @block.vector
        def _(dve):
            done = [0]

            def link(ins):
                done[0] += 1
                ins.then_inc(prep, 1)
                dve.wait_ge(prep, done[0])

            link(nc.vector.memset(ones, 1.0))
            dve.wait_ge(ids_in, 32)
            link(nc.vector.tensor_copy(ids_f, ids_i))
            dve.wait_ge(consts_in, 16)
            link(nc.vector.tensor_scalar(hot, ids_f, con[0:WEIGHTS, CAT:CAT + 1], None, ALU.is_equal))
            link(nc.vector.tensor_tensor(scored, hot, con[0:WEIGHTS, SCORE:SCORE + BATCHES], ALU.mult))
            link(nc.vector.reduce_max(best, scored, AX.X))
            link(nc.vector.tensor_scalar(key, best, float(P), con[0:WEIGHTS, TIE:TIE + 1],
                                         ALU.mult, ALU.add))
            dve.wait_ge(eye_in, 16)
            link(nc.vector.tensor_scalar(diag, ident[0:WEIGHTS, 0:WEIGHTS], key, None, ALU.mult))
            link(nc.vector.tensor_scalar(needed, con[0:WEIGHTS, NEED:NEED + 2 * PAIRS], key, None,
                                         ALU.is_le))
            dve.wait_ge(keys_out, 1)
            link(nc.vector.tensor_scalar(later, ps_keys, key, None, ALU.is_gt))
            link(nc.vector.reduce_sum(rank, later, AX.X))
            link(nc.vector.tensor_scalar(placed, con[0:WEIGHTS, IOTA:IOTA + WEIGHTS], rank, None,
                                         ALU.is_equal))
            link(nc.vector.tensor_scalar(rank2, con[0:WEIGHTS, MASK:MASK + 2], rank, None, ALU.mult))
            dve.wait_ge(order_out, 1)
            nc.vector.tensor_copy(order[:, :], ps_order).then_inc(order_ready, 1)
            dve.wait_ge(table_out, 1)
            nc.vector.tensor_copy(table[:, :], ps[0:1, 1, 0:PAIRS * ENTRY]).then_inc(table_ready, 1)
            dve.wait_ge(pick_in, 16)
            link(nc.vector.tensor_copy(pick_b[:, :], pick_f))
            dve.wait_ge(b0_out, 1)
            nc.vector.tensor_copy(b0_t[:, :, :], ps_b0).then_inc(b0_ready, 1)
            dve.wait_ge(b_out, 1)
            link(nc.vector.tensor_copy(b_sum[:, :, :], ps_b))
            for rows in (slice(32, 64), slice(64, 96)):
                link(nc.vector.tensor_tensor(ps_b[rows], ps_b[rows], b_sum[rows], ALU.subtract))
                link(nc.vector.tensor_copy(b_sum[rows], ps_b[rows]))
            link(nc.vector.tensor_tensor(ps_b[rows], ps_b[rows], b_sum[rows], ALU.subtract))
            nc.vector.tensor_copy(b_sum[rows], ps_b[rows]).then_inc(b_ready, 1)

            def copy_w0(r, n):
                at = r * (STEP * ENTRY) + n * ENTRY
                need = dve.value_load(table[0:1, ds(at, 1)], min_val=1, max_val=WEIGHTS)
                place = dve.value_load(table[0:1, ds(at + 4, 1)], min_val=0, max_val=WEIGHTS - 1)
                dve.wait_ge(w_here, need)
                nc.vector.tensor_copy(w0_b[:, n % 2:n % 2 + 1, :], w_all[:, ds(place, 1), :]
                                      ).then_inc(w0b_ready, 1)

            def result(r, n):
                dve.wait_ge(l2_done, r * STEP + (n + 1))
                if n % GROUP == 0 and not (isinstance(r, int) and r == 0):
                    dve.wait_ge(o_gone[n // GROUP], r * 16)
                nc.vector.tensor_tensor(o[:, n, :], ps_2[:, n % 2, :], z[:, n, :], ALU.add
                                        ).then_inc(o_ready, 1)

            def step(r, n):
                dve.wait_ge(l1_done, r * STEP + (n + 1))
                nc.vector.tensor_tensor(z[:, n, :], ps_1[:, n % 2, :], x_in[:, n, :], ALU.add
                                        ).then_inc(z_ready, 1)
                if not is_pair(r, n, PAIRS - 1):
                    copy_w0(*pair(r, n, 1))
                if not is_pair(r, n, 0):
                    result(*pair(r, n, -1))
                dve.wait_ge(tz_done, r * STEP + (n + 1))
                bias = b0_t[:, :, ds(r * (2 * STEP) + 2 * n, 2)]
                nc.vector.tensor_tensor(
                    y_t[:, n % 2, :, :].rearrange("p t (h c) -> p t h c", h=2),
                    ps_z[:, n % 2, :].rearrange("p (t h c) -> p t h c", t=CHUNKS, h=2),
                    bias.unsqueeze(3).to_broadcast([P, CHUNKS, 2, TOK]), ALU.add
                    ).then_inc(yt_ready, 1)

            dve.wait_ge(table_ready, 1)
            copy_w0(0, 0)
            whole(dve, step)
            result(ROUNDS - 1, STEP - 1)

        @block.scalar
        def _(act):
            def load_x(g, slot):
                act.dma_start(x_in[:, GROUP * slot:GROUP * slot + GROUP, :],
                              x_d[ds(g, 1)].rearrange("g p k f -> p (g k) f")
                              ).then_inc(x_here[slot], 16)

            def store(g, slot):
                act.dma_start(out_d[ds(g, 1)].rearrange("g p k f -> p (g k) f"),
                              o[:, GROUP * slot:GROUP * slot + GROUP, :]
                              ).then_inc(o_gone[slot], 16)

            def evict_x(r, n):
                act.wait_ge(tx_done, r * STEP + (n + 1))
                nc.scalar.copy(x_t[:, n % 2, :, :].rearrange("p t c -> p (t c)"),
                               ps_x[:, n % 2, :]).then_inc(xt_ready, 1)

            def copy_w1(r, n):
                at = r * (STEP * ENTRY) + n * ENTRY
                need = act.value_load(table[0:1, ds(at + 1, 1)], min_val=1, max_val=WEIGHTS)
                place = act.value_load(table[0:1, ds(at + 5, 1)], min_val=0, max_val=WEIGHTS - 1)
                act.wait_ge(w_here, need)
                nc.scalar.copy(pick[:, n % 2, :].rearrange("p (h c) -> p h c", h=2),
                               pick_b[:, ds((r % 4) * (2 * STEP) + 2 * n, 2)]
                               .unsqueeze(2).to_broadcast([96, 2, TOK]))
                nc.scalar.copy(w1_b[:, n % 2:n % 2 + 1, :], w_all[:, ds(place, 1), :]
                               ).then_inc(w1b_ready, 1)

            act.dma_start(ident[:, :], eye[:, :]).then_inc(eye_in, 16)
            load_x(0, 0)
            load_x(1, 1)
            evict_x(0, 0)
            act.wait_ge(table_ready, 1)
            act.wait_ge(prep, 13)

            def step(r, n):
                if not is_pair(r, n, PAIRS - 1):
                    evict_x(*pair(r, n, 1))
                else:
                    act.wait_ge(l2_done, PAIRS - 2)
                copy_w1(r, n)
                if n % 2:
                    slot = n // 2
                    if not (isinstance(r, int) and r == ROUNDS - 1):
                        act.wait_ge(z_ready, r * STEP + (n + 1))
                        load_x(r * 2 + (slot + 2), slot)
                    if not is_pair(r, n, 1):
                        act.wait_ge(o_ready, r * STEP + (n - 1))
                        store(r * 2 + (slot - 1), 1 - slot)

            whole(act, step)
            act.wait_ge(o_ready, PAIRS)
            store(GROUPS - 1, 1)
            for slot in range(2):
                act.wait_ge(o_gone[slot], 16 * (GROUPS // 2))


def kernel(x, itok_B_0_30, itok_B_0_63, L0_cond_W, L0_cond_b, L1_cond_W, L1_cond_b):
    import concourse.bacc as _bacc
    from concourse.bass_utils import run_bass_kernel_spmd as _run

    consts, eye, pick = constants()
    arrays = {
        "x": np.ascontiguousarray(x),
        "ids0": np.ascontiguousarray(itok_B_0_30),
        "ids1": np.ascontiguousarray(itok_B_0_63),
        "weights": np.concatenate([L1_cond_W, L0_cond_W]),
        "biases": np.concatenate([L1_cond_b, L0_cond_b]),
        "consts": consts, "eye": eye, "picks": pick,
    }
    nc = _bacc.Bacc("TRN2", target_bir_lowering=False, num_devices=1, dynamic_dma_scratch_size=1024)
    args = [nc.dram_tensor(name, a.shape, mybir.dt.from_np(a.dtype), kind="ExternalInput").ap()
            for name, a in arrays.items()]
    out = nc.dram_tensor("out", [BATCHES, TOK, DIM], mybir.dt.float32, kind="ExternalOutput").ap()
    two_layers(nc, *args, out)
    return _run(nc, [arrays], core_ids=[0]).results[0]["out"]
```
